# Optimizing a Trainium2 kernel written in Bass

```python
import numpy as np
import jax
import jax.numpy as jnp

def _softmax(x, axis=-1):
    return jax.nn.softmax(x, axis=axis)

def _gelu(x):
    return jax.nn.gelu(x, approximate=True)

def _silu(x):
    return jax.nn.silu(x)

def _sigmoid(x):
    return jax.nn.sigmoid(x)

def _layernorm(x, axis=-1, eps=1e-05):
    m = jnp.mean(x, axis=axis, keepdims=True)
    v = jnp.var(x, axis=axis, keepdims=True)
    return (x - m) / jnp.sqrt(v + eps)

def _scatter_add(tgt, idx, src, axis=0):
    return tgt.at[idx].add(src)

def _segment_sum(src, seg, n):
    return jax.ops.segment_sum(src, seg, n)
kernel_name = 'mk_adj_resnorm_d1_adj_r2_5202cc'

def setup_inputs(seed: int=0):
    np.random.seed(seed)
    _w = jnp.asarray

    def _rec_inputs():
        import jax
        import jax.numpy as jnp
        _gk = jax.random.key(seed)
        x = -0.0001538 + 1 * jax.random.normal(jax.random.fold_in(_gk, 1), (128, 128, 384), jnp.float32)
        _a = jax.random.bernoulli(jax.random.fold_in(_gk, 2), 0.03125, (128, 128, 128))
        _a = jnp.logical_or(_a, jnp.swapaxes(_a, -1, -2))
        _a = jnp.logical_or(_a, jnp.eye(128, dtype=bool))
        _af = _a.astype(jnp.float32)
        _af = _af * jax.random.uniform(jax.random.fold_in(_gk, 3), (128, 128, 128), jnp.float32, 0.05, 5.06092)
        adj = _af
        return (x, adj)
    x, adj = _rec_inputs()

    def _L0_gnn_setup():
        import jax, jax.numpy as jnp
        import numpy as np
        D_MODEL = 384
        NHEADS = 8
        D_FF = 1536
        B, N = (8, 512)
        EPS = 1e-06

        def _rmsnorm(x, alpha, gamma):
            x = x * jax.lax.rsqrt(jnp.mean(x * x, axis=-1, keepdims=True) + EPS)
            return alpha * x + gamma
        key = jax.random.key(seed)
        ks = jax.random.split(key, 10)
        d, f = (D_MODEL, D_FF)
        s = 1.0 / np.sqrt(d)
        inp = {'x': jax.random.normal(ks[0], (B, N, d), dtype=jnp.float32), 'attn_bias': jax.random.normal(ks[1], (B, N, N), dtype=jnp.float32), 'wq': jax.random.normal(ks[2], (d, d), dtype=jnp.float32) * s, 'bq': jnp.zeros((d,), jnp.float32), 'wk': jax.random.normal(ks[3], (d, d), dtype=jnp.float32) * s, 'bk': jnp.zeros((d,), jnp.float32), 'wv': jax.random.normal(ks[4], (d, d), dtype=jnp.float32) * s, 'bv': jnp.zeros((d,), jnp.float32), 'wo': jax.random.normal(ks[5], (d, d), dtype=jnp.float32) * s, 'bo': jnp.zeros((d,), jnp.float32), 'w1': jax.random.normal(ks[6], (d, f), dtype=jnp.float32) * s, 'b1': jnp.zeros((f,), jnp.float32), 'w2': jax.random.normal(ks[7], (f, d), dtype=jnp.float32) * (1.0 / np.sqrt(f)), 'b2': jnp.zeros((d,), jnp.float32), 'alpha1': jnp.ones((d,), jnp.float32), 'gamma1': jnp.ones((d,), jnp.float32), 'alpha2': jnp.ones((d,), jnp.float32), 'gamma2': jnp.ones((d,), jnp.float32)}
        return inp
    _L0_gnn_all = _L0_gnn_setup()
    _L0_gnn_in = {k: v for k, v in _L0_gnn_all.items() if k in ('wq', 'bq', 'wk', 'bk', 'wv', 'bv', 'wo', 'bo', 'w1', 'b1', 'w2', 'b2', 'alpha1', 'gamma1', 'alpha2', 'gamma2')}
    del _L0_gnn_all
    return {'x': x, 'adj': adj, 'L0_gnn_wq': _L0_gnn_in['wq'], 'L0_gnn_bq': _L0_gnn_in['bq'], 'L0_gnn_wk': _L0_gnn_in['wk'], 'L0_gnn_bk': _L0_gnn_in['bk'], 'L0_gnn_wv': _L0_gnn_in['wv'], 'L0_gnn_bv': _L0_gnn_in['bv'], 'L0_gnn_wo': _L0_gnn_in['wo'], 'L0_gnn_bo': _L0_gnn_in['bo'], 'L0_gnn_w1': _L0_gnn_in['w1'], 'L0_gnn_b1': _L0_gnn_in['b1'], 'L0_gnn_w2': _L0_gnn_in['w2'], 'L0_gnn_b2': _L0_gnn_in['b2'], 'L0_gnn_alpha1': _L0_gnn_in['alpha1'], 'L0_gnn_gamma1': _L0_gnn_in['gamma1'], 'L0_gnn_alpha2': _L0_gnn_in['alpha2'], 'L0_gnn_gamma2': _L0_gnn_in['gamma2']}

def reference(x, adj, L0_gnn_wq, L0_gnn_bq, L0_gnn_wk, L0_gnn_bk, L0_gnn_wv, L0_gnn_bv, L0_gnn_wo, L0_gnn_bo, L0_gnn_w1, L0_gnn_b1, L0_gnn_w2, L0_gnn_b2, L0_gnn_alpha1, L0_gnn_gamma1, L0_gnn_alpha2, L0_gnn_gamma2):
    import jax
    import jax.numpy as jnp

    def _L0_gnn_ref(x, attn_bias, wq, bq, wk, bk, wv, bv, wo, bo, w1, b1, w2, b2, alpha1, gamma1, alpha2, gamma2):
        import jax, jax.numpy as jnp
        import numpy as np
        D_MODEL = 384
        NHEADS = 8
        D_FF = 1536
        B, N = (8, 512)
        EPS = 1e-06

        def _rmsnorm(x, alpha, gamma):
            x = x * jax.lax.rsqrt(jnp.mean(x * x, axis=-1, keepdims=True) + EPS)
            return alpha * x + gamma
        b, n, d = x.shape
        h = NHEADS
        dh = d // h
        scaling = dh ** (-0.5)

        def split_heads(t):
            return t.reshape(b, n, h, dh).transpose(0, 2, 1, 3)
        q = split_heads(x @ wq + bq)
        k = split_heads(x @ wk + bk)
        v = split_heads(x @ wv + bv)
        scores = jnp.einsum('bhqd,bhkd->bhqk', q, k) * scaling
        scores = scores + attn_bias[:, None, :, :]
        attn = jax.nn.softmax(scores, axis=-1)
        ctx = jnp.einsum('bhij,bhjd->bhid', attn, v)
        ctx = ctx.transpose(0, 2, 1, 3).reshape(b, n, d)
        attn_out = ctx @ wo + bo
        x = _rmsnorm(x + attn_out, alpha1, gamma1)
        ff = jax.nn.silu(x @ w1 + b1) @ w2 + b2
        x = _rmsnorm(x + ff, alpha2, gamma2)
        return x
    x = _layernorm(x + _L0_gnn_ref(x, adj, L0_gnn_wq, L0_gnn_bq, L0_gnn_wk, L0_gnn_bk, L0_gnn_wv, L0_gnn_bv, L0_gnn_wo, L0_gnn_bo, L0_gnn_w1, L0_gnn_b1, L0_gnn_w2, L0_gnn_b2, L0_gnn_alpha1, L0_gnn_gamma1, L0_gnn_alpha2, L0_gnn_gamma2), axis=-1)
    return x

_drawn_inputs = setup_inputs


def setup_inputs(seed=0):
    import zlib

    import numpy as np

    out = dict(_drawn_inputs(seed))
    spreads = {'L0_gnn_bq': (0.0, 0.721),
     'L0_gnn_bk': (0.0, 0.8),
     'L0_gnn_bv': (0.0, 0.1),
     'L0_gnn_bo': (0.0, 0.1),
     'L0_gnn_b1': (0.0, 0.338),
     'L0_gnn_b2': (0.0, 0.1),
     'L0_gnn_alpha1': (1.0, 0.2),
     'L0_gnn_gamma1': (1.0, 0.2),
     'L0_gnn_alpha2': (1.0, 0.2),
     'L0_gnn_gamma2': (1.0, 0.2)}
    factors = {}
    for name, (base, spread) in spreads.items():
        noise = np.random.default_rng([zlib.crc32(name.encode()), seed]).standard_normal(out[name].shape)
        drawn = base * np.exp(spread * noise) if base else spread * noise
        out[name] = jnp.asarray(drawn.astype(out[name].dtype))
    for name, factor in factors.items():
        out[name] = (out[name] * factor).astype(out[name].dtype)
    return out
```

```python
from contextlib import ExitStack

import concourse.bass as bass
from concourse import mybir

F32 = mybir.dt.float32
F32R = mybir.dt.float32r
ALU = mybir.AluOpType
ACT = mybir.ActivationFunctionType
AX = mybir.AxisListType

P = 128
PAIR = 2
HEADS = 8
HALF = 64
HI, LO = 0, 1
PASSES = ((LO, HI), (HI, LO), (HI, HI))
RMS_EPS = 1e-6
LN_EPS = 1e-5
STAGE_SLOTS = 3
STAGE_COLS = 768
LAG_PROJ, LAG_ATTN, LAG_FF1, LAG_FF2 = 1, 2, 3, 4


def build_layer(nc, x, adj, wq, bq, wk, bk, wv, bv, wo, bo, w1, b1, w2, b2,
                alpha1, gamma1, alpha2, gamma2, out):
    graphs, nodes, d = x.shape
    f = w1.shape[1]
    groups = graphs // PAIR
    toks = PAIR * nodes
    dh = d // HEADS
    kd = d // P
    hp = HEADS // 2
    fc = f // P
    scale = float(dh) ** -0.5
    slots = groups + LAG_FF2
    loop_from, loop_to = LAG_FF2 + 2, groups
    assert nodes == P and loop_from % 2 == 0 and loop_to % 2 == 0 and dh <= HALF

    ctx = ExitStack()
    with ctx:
        def sb(name, shape, dt=F32):
            return ctx.enter_context(nc.sbuf_tensor(name, shape, dt))

        def ps(name, cols):
            return ctx.enter_context(nc.psum_tensor(name, [P, cols], F32))

        def sem(name):
            return ctx.enter_context(nc.semaphore(name))

        def sems(name, n):
            return [sem(f"{name}{i}") for i in range(n)]

        ctx.enter_context(nc.allow_non_contiguous_dma(reason="biases laid out by partition, once"))

        wq_s = sb("wq_s", [P, 2, kd, hp * P], F32R)
        wk_s = sb("wk_s", [P, 2, kd, hp * P], F32R)
        wv_s = sb("wv_s", [P, 2, kd, d], F32R)
        wo_s = sb("wo_s", [P, 2, hp, d], F32R)
        w1_s = sb("w1_s", [P, 2, kd, f], F32R)
        w2_s = sb("w2_s", [P, 2, fc, d], F32R)
        stage = sb("stage", [P, STAGE_SLOTS, STAGE_COLS])
        bq_col = sb("bq_col", [P, hp])
        bk_col = sb("bk_col", [P, hp])
        b1_col = sb("b1_col", [P, fc])
        rows = sb("rows", [P, 7, d])
        BO, BV, B2, ALPHA1, GAMMA1, ALPHA2, GAMMA2 = range(7)
        ident = sb("ident", [P, P])
        neg_half = sb("neg_half", [P, 1])
        x_in = sb("x_in", [P, PAIR, d])
        x_res = sb("x_res", [P, PAIR, d])
        x_last = sb("x_last", [P, PAIR, d])
        bias = sb("bias", [P, 2, PAIR, P])
        xT = sb("xT", [P, 2, kd, toks], F32R)
        q = sb("q", [P, hp, toks])
        k = sb("k", [P, hp, toks])
        v = sb("v", [P, PAIR, HEADS, HALF])
        probs = sb("probs", [P, PAIR, HEADS, P])
        neg_max = sb("neg_max", [P, PAIR, HEADS])
        row_sum = sb("row_sum", [P, PAIR, HEADS])
        row_inv = sb("row_inv", [P, PAIR, HEADS])
        ctxT = sb("ctxT", [P, 2, hp, P], F32R)
        x1 = sb("x1", [P, 2, PAIR, d])
        x1T = sb("x1T", [P, 2, kd, toks], F32R)
        h_raw = sb("h_raw", [P, 2, 2 * toks])
        h = sb("h", [P, 2, fc, toks], F32R)
        y = sb("y", [P, PAIR, d])
        squares = stage[:, 0, 0:d]
        sum_sq1 = sb("sum_sq1", [P, PAIR])
        sum_sq2 = sb("sum_sq2", [P, PAIR])
        mean_sq1 = sb("mean_sq1", [P, PAIR])
        mean_sq2 = sb("mean_sq2", [P, PAIR])
        inv_rms1 = sb("inv_rms1", [P, PAIR])
        inv_rms2 = sb("inv_rms2", [P, PAIR])
        stats = sb("stats", [P, PAIR, 6])
        mean_var = sb("mean_var", [P, PAIR, 2])
        var_eps = sb("var_eps", [P, PAIR])
        inv_std = sb("inv_std", [P, PAIR])

        ps_scores = ps("ps_scores", HEADS * P)
        ps_probsT = ps("ps_probsT", HEADS * P)
        ps_ctx = ps("ps_ctx", hp * P)
        ps_rows = ps("ps_rows", 512)
        ps_work = [ps("ps_work0", 512), ps("ps_work1", 512)]

        stage_loaded = sems("stage_loaded", STAGE_SLOTS)
        weight_hi = sem("weight_hi")
        weight_split = sem("weight_split")
        vectors_loaded = sem("vectors_loaded")
        pads_zeroed = sem("pads_zeroed")
        cols_zeroed = sem("cols_zeroed")
        bq_scaled = sem("bq_scaled")
        ident_zeroed = sem("ident_zeroed")
        ident_ready = sem("ident_ready")
        x_in_loaded = sem("x_in_loaded")
        x_res_loaded = sem("x_res_loaded")
        x_last_loaded = sem("x_last_loaded")
        bias_loaded = sems("bias_loaded", 2)
        y_stored = sem("y_stored")
        xT_done = sems("xT_done", 2)
        xT_hi = sems("xT_hi", 2)
        xT_lo = sems("xT_lo", 2)
        q_done, q_ready = sems("q_done", 2), sems("q_ready", 2)
        k_done, k_ready = sems("k_done", 2), sems("k_ready", 2)
        v_done, v_ready = sems("v_done", PAIR), sems("v_ready", PAIR)
        scores_done = sems("scores_done", PAIR)
        scores_biased = sems("scores_biased", PAIR)
        max_ready = sems("max_ready", PAIR)
        exp_ready = sems("exp_ready", PAIR)
        inv_ready = sems("inv_ready", PAIR)
        probs_ready = sems("probs_ready", PAIR)
        probsT_done = sems("probsT_done", PAIR)
        probsT_ready = sems("probsT_ready", PAIR)
        ctx_done = sems("ctx_done", PAIR)
        ctx_hi = sems("ctx_hi", PAIR)
        ctx_lo = sems("ctx_lo", PAIR)
        attn_done = sems("attn_done", PAIR)
        x_res_biased = sem("x_res_biased")
        res1_ready = sems("res1_ready", PAIR)
        sq1_ready = sems("sq1_ready", PAIR)
        ms1_ready = sems("ms1_ready", PAIR)
        rms1_ready = sems("rms1_ready", PAIR)
        x1_scaled = sems("x1_scaled", PAIR)
        x1_ready = sems("x1_ready", PAIR)
        x1_b2_ready = sem("x1_b2_ready")
        x1T_done = sems("x1T_done", 2)
        x1T_hi = sems("x1T_hi", 2)
        x1T_lo = sems("x1T_lo", 2)
        up_done = sems("up_done", fc // 2)
        silu_ready = sems("silu_ready", fc // 2)
        h_hi = sems("h_hi", fc // 2)
        h_lo = sems("h_lo", fc // 2)
        down_done = sems("down_done", PAIR)
        x_last_biased = sem("x_last_biased")
        res2_ready = sems("res2_ready", PAIR)
        sq2_ready = sems("sq2_ready", PAIR)
        ms2_ready = sems("ms2_ready", PAIR)
        rms2_ready = sems("rms2_ready", PAIR)
        y_scaled = sems("y_scaled", PAIR)
        y_summed = sems("y_summed", PAIR)
        stats_ready = sems("stats_ready", PAIR)
        var_ready = sems("var_ready", PAIR)
        var_eps_ready = sems("var_eps_ready", PAIR)
        std_ready = sems("std_ready", PAIR)
        y_ready = sems("y_ready", PAIR)

        units = []

        def unit(src, dst, cols, lo_p=0, n_p=P, inner=None):
            slot = len(units) % STAGE_SLOTS
            at = stage[lo_p:lo_p + n_p, slot, 0:cols]
            if inner:
                at = at.rearrange("p (a b) -> p a b", b=inner)
            units.append((src, at, dst(HI), dst(LO), slot))

        for w_dram, w_sb in ((wq, wq_s), (wk, wk_s)):
            for kb in range(kd):
                unit(w_dram[kb * P:(kb + 1) * P, :].rearrange("p (h e) -> p h e", e=dh),
                     lambda part, w_sb=w_sb, kb=kb: w_sb[:, part, kb, :].rearrange(
                         "p (h e) -> p h e", e=HALF)[:, :, 0:dh], d, inner=dh)
        for kb in range(kd):
            unit(wv[kb * P:(kb + 1) * P, :], lambda part, kb=kb: wv_s[:, part, kb, :], d)
        proj_units = len(units)
        wo_rows = wo.rearrange("(c two e) n -> two e c n", two=2, e=dh)
        for side in range(2):
            for c in range(0, hp, 2):
                unit(wo_rows[side, :, c:c + 2, :],
                     lambda part, side=side, c=c: wo_s[side * HALF:side * HALF + dh, part, c:c + 2, :],
                     2 * d, side * HALF, dh, d)
        out_units = len(units)
        for kb in range(kd):
            for n in range(0, f, STAGE_COLS):
                unit(w1[kb * P:(kb + 1) * P, n:n + STAGE_COLS],
                     lambda part, kb=kb, n=n: w1_s[:, part, kb, n:n + STAGE_COLS], STAGE_COLS)
        up_units = len(units)
        w2_rows = w2.rearrange("(m p) n -> p m n", p=P)
        for m in range(0, fc, 2):
            unit(w2_rows[:, m:m + 2, :], lambda part, m=m: w2_s[:, part, m:m + 2, :], 2 * d, inner=d)
        n_units = len(units)

        n_vectors = 12

        def place(head):
            return head % 2 * hp + head // 2

        def static(g):
            return isinstance(g, int)

        def live(g):
            return not static(g) or 0 <= g < groups

        def after(engine, semaphore, g, each=1):
            if static(g) and g < 0:
                return
            engine.wait_ge(semaphore, (g + 1) * each)

        def after_apart(engine, semaphore, g):
            engine.wait_ge(vectors_loaded, 16 * n_vectors)
            after(engine, semaphore, g)

        def run_slots(engine, slot):
            for t in range(loop_from):
                slot(t, t % 2)
            with engine.Fori(loop_from // 2, loop_to // 2) as two_slots:
                slot(two_slots * 2, 0)
                slot(two_slots * 2 + 1, 1)
            for t in range(loop_to, slots):
                slot(t, t % 2)

        def group_rows(ap, g):
            if static(g):
                return ap[g * PAIR:(g + 1) * PAIR].rearrange("b n e -> n b e")
            return ap[bass.ds(g * PAIR, PAIR)].rearrange("b n e -> n b e")

        block = ctx.enter_context(nc.Block())

        @block.sync
        def _(sp):
            sp.wait_ge(cols_zeroed, 1)
            for col, src in ((bq_col, bq), (bk_col, bk)):
                by_side = src.rearrange("(c two e) -> two e c", two=2, e=dh)
                for side in range(2):
                    sp.dma_start(col[side * HALF:side * HALF + dh, :],
                                 by_side[side]).then_inc(vectors_loaded, 16)
            sp.dma_start(b1_col[:], b1.rearrange("(m p) -> p m", p=P)).then_inc(vectors_loaded, 16)
            for i, row in enumerate((bo, bv, b2, alpha1, gamma1, alpha2, gamma2)):
                sp.dma_start(rows[:, i, :], row.partition_broadcast(P)).then_inc(vectors_loaded, 16)
            for n, (src, at, _, _, slot) in enumerate(units):
                if n >= STAGE_SLOTS:
                    sp.wait_ge(weight_split, n - STAGE_SLOTS + 1)
                sp.dma_start(at, src).then_inc(stage_loaded[slot], 16)

            def slot_program(t, parity):
                g = t
                if live(g):
                    for i in range(2):
                        after(sp, xT_done[i], g - 1)
                    sp.dma_start(x_in[:], group_rows(x, g)).then_inc(x_in_loaded, 16)
                g = t - LAG_ATTN
                if live(g):
                    for b in range(PAIR):
                        after(sp, res1_ready[b], g - 1)
                    sp.dma_start(x_res[:], group_rows(x, g)).then_inc(x_res_loaded, 16)
                g = t - LAG_PROJ
                if live(g):
                    after(sp, scores_biased[PAIR - 1], g - 2)
                    sp.dma_start(bias[:, 1 - parity],
                                 group_rows(adj, g)).then_inc(bias_loaded[1 - parity], 16)
                g = t - LAG_FF1
                if live(g):
                    for b in range(PAIR):
                        after(sp, y_summed[b], g - 1)
                    sp.dma_start(x_last[:], group_rows(x, g)).then_inc(x_last_loaded, 16)
                g = t - LAG_FF2
                if live(g):
                    for b in range(PAIR):
                        after(sp, y_ready[b], g)
                    sp.dma_start(group_rows(out, g), y[:]).then_inc(y_stored, 16)

            run_slots(sp, slot_program)
            sp.wait_ge(y_stored, 16 * groups)

        @block.gpsimd
        def _(pool):
            pool.memset(bq_col[:], 0.0)
            pool.memset(bk_col[:], 0.0).then_inc(cols_zeroed, 1)
            for w in (wq_s, wk_s, wo_s):
                pool.memset(w[:].bitcast(F32), 0.0)
            pool.memset(v[:], 0.0)
            pool.memset(neg_half[:], -0.5).then_inc(pads_zeroed, 1)
            pool.memset(ident[:], 0.0).then_inc(ident_zeroed, 1)
            pool.wait_ge(ident_zeroed, 1)
            pool.affine_select(out=ident[:], in_=ident[:], compare_op=ALU.not_equal, fill=1.0, base=0,
                               pattern=[[-1, P]], channel_multiplier=1).then_inc(ident_ready, 1)
            pool.wait_ge(vectors_loaded, 16 * n_vectors)
            pool.wait_ge(pads_zeroed, 1)

            def row(i):
                return rows[:, i, :].unsqueeze(1).to_broadcast([P, PAIR, d])

            def inverse_root(b, source, s_source, g, times, eps, shifted, s_shifted, result, s_result):
                after_apart(pool, s_source[b], g)
                pool.tensor_scalar(shifted[:, b:b + 1], source, times, eps, ALU.mult,
                                   ALU.add).then_inc(s_shifted[b], 1)
                after(pool, s_shifted[b], g)
                pool.tensor_tensor(result[:, b:b + 1], shifted[:, b:b + 1], neg_half[:],
                                   ALU.pow).then_inc(s_result[b], 1)

            def slot_program(t, parity):
                g_ff2 = t - LAG_FF2
                g_attn = t - LAG_ATTN
                if live(g_ff2):
                    after(pool, x_last_loaded, g_ff2, 16)
                    pool.tensor_tensor(x_last[:], x_last[:], row(GAMMA2),
                                       ALU.add).then_inc(x_last_biased, 1)
                if live(g_attn):
                    after(pool, x_res_loaded, g_attn, 16)
                    pool.tensor_tensor(x_res[:], x_res[:], row(BO), ALU.add).then_inc(x_res_biased, 1)
                if live(g_ff2):
                    for b in range(PAIR):
                        inverse_root(b, sum_sq2[:, b:b + 1], sq2_ready, g_ff2, 1.0 / d, RMS_EPS,
                                     mean_sq2, ms2_ready, inv_rms2, rms2_ready)
                        inverse_root(b, mean_var[:, b, 1:2], var_ready, g_ff2, 1.0, LN_EPS,
                                     var_eps, var_eps_ready, inv_std, std_ready)
                if live(g_attn):
                    for b in range(PAIR):
                        inverse_root(b, sum_sq1[:, b:b + 1], sq1_ready, g_attn, 1.0 / d, RMS_EPS,
                                     mean_sq1, ms1_ready, inv_rms1, rms1_ready)
                    for i in range(2):
                        after(pool, x1T_done[i], g_attn)
                    pool.tensor_tensor(x1[:, parity], x1[:, parity], row(B2),
                                       ALU.add).then_inc(x1_b2_ready, 1)

            run_slots(pool, slot_program)

        @block.tensor
        def _(pe):
            def passes(ps_out, pairs):
                n = len(PASSES) * len(pairs)
                i = 0
                for sta, mov in PASSES:
                    for stationary, moving in pairs:
                        mm = pe.matmul(ps_out, stationary(sta), moving(mov), start=(i == 0), stop=(i == n - 1))
                        i += 1
                return mm

            def scores(g, b):
                if b == 0:
                    for i in range(2):
                        after(pe, q_ready[i], g)
                        after(pe, k_ready[i], g)
                    after(pe, scores_biased[PAIR - 1], g - 1)
                else:
                    after(pe, scores_biased[b - 1], g)
                for head in range(HEADS):
                    c, p0 = head // 2, head % 2 * HALF
                    at = place(head) * P
                    mm = pe.matmul(ps_scores[:, at:at + P],
                                   q[p0:p0 + dh, c, b * P:(b + 1) * P], k[p0:p0 + dh, c, b * P:(b + 1) * P],
                                   start=True, stop=True)
                mm.then_inc(scores_done[b], 1)

            def transpose_probs(g, b):
                after(pe, probs_ready[b], g)
                after(pe, probsT_ready[PAIR - 1 if b == 0 else b - 1], g - 1 if b == 0 else g)
                for head in range(HEADS):
                    mm = pe.transpose(ps_probsT[:, head * P:(head + 1) * P], probs[:, b, head, :], ident[:])
                mm.then_inc(probsT_done[b], 1)

            def context(g, b):
                after(pe, probsT_ready[b], g)
                after(pe, v_ready[b], g)
                after(pe, ctx_lo[PAIR - 1 if b == 0 else b - 1], g - 1 if b == 0 else g)
                for head in range(HEADS):
                    c, p0 = head // 2, head % 2 * HALF
                    mm = pe.matmul(ps_ctx[p0:p0 + HALF, c * P:(c + 1) * P], v[:, b, head, :],
                                   probs[:, b, place(head), :], start=True, stop=True)
                mm.then_inc(ctx_done[b], 1)

            def output_product(g, b):
                after(pe, ctx_lo[b], g)
                if b:
                    after(pe, res1_ready[b - 1], g)
                elif live(g - LAG_FF2 + LAG_ATTN):
                    after(pe, res2_ready[PAIR - 1], g - LAG_FF2 + LAG_ATTN)
                else:
                    after(pe, res1_ready[PAIR - 1], g - 1)
                passes(ps_rows[:, 0:d], [
                    (lambda part, c=c: ctxT[:, part, c, :], lambda part, c=c: wo_s[:, part, c, :])
                    for c in range(hp)]).then_inc(attn_done[b], 1)

            def down(g, b):
                if b == 0:
                    for i in range(fc // 2):
                        after(pe, h_lo[i], g)
                    if live(g + LAG_FF2 - LAG_ATTN - 1):
                        after(pe, res1_ready[PAIR - 1], g + LAG_FF2 - LAG_ATTN - 1)
                    else:
                        after(pe, res2_ready[PAIR - 1], g - 1)
                else:
                    after(pe, res2_ready[b - 1], g)
                passes(ps_rows[:, 0:d], [
                    (lambda part, m=m: h[:, part, m, b * P:(b + 1) * P], lambda part, m=m: w2_s[:, part, m, :])
                    for m in range(fc)]).then_inc(down_done[b], 1)

            def project(w, ps_out, c, last):
                mm = passes(ps_out, [
                    (lambda part, kb=kb: w[:, part, kb, c * P:(c + 1) * P], lambda part, kb=kb: xT[:, part, kb, :])
                    for kb in range(kd)])
                if last is not None:
                    mm.then_inc(last, 1)

            def project_qk(g):
                for i in range(2):
                    after(pe, xT_lo[i], g)
                for i in range(2):
                    after(pe, x1T_lo[i], g - LAG_ATTN + LAG_PROJ - 1)
                    for j in range(2):
                        project(wq_s, ps_work[i][:, j * toks:(j + 1) * toks], 2 * i + j, q_done[i] if j else None)
                for i in range(2):
                    after(pe, q_ready[i], g)
                    for j in range(2):
                        project(wk_s, ps_work[i][:, j * toks:(j + 1) * toks], 2 * i + j, k_done[i] if j else None)

            def project_v(g):
                for b in range(PAIR):
                    after(pe, k_ready[b], g)
                    passes(ps_work[b][:, 0:d], [
                        (lambda part, kb=kb: xT[:, part, kb, b * P:(b + 1) * P],
                         lambda part, kb=kb: wv_s[:, part, kb, :]) for kb in range(kd)]).then_inc(v_done[b], 1)

            def transpose_rows(rows_in, done):
                for i, blocks in enumerate(((0, 1), (2,))):
                    yield i
                    for kb in blocks:
                        for b in range(PAIR):
                            at = kb % 2 * toks + b * P
                            mm = pe.transpose(ps_work[i][:, at:at + P], rows_in[:, b, kb * P:(kb + 1) * P], ident[:])
                    mm.then_inc(done[i], 1)

            def transpose_x(g):
                after(pe, x_in_loaded, g, 16)
                for i in transpose_rows(x_in, xT_done):
                    if live(g - LAG_PROJ):
                        after(pe, v_ready[i], g - LAG_PROJ)

            def up(g):
                for i in range(2):
                    after(pe, x1T_lo[i], g)
                for m in range(fc // 2):
                    if m >= 2:
                        after(pe, silu_ready[m - 2], g)
                    elif live(g + LAG_FF1):
                        after(pe, xT_lo[m], g + LAG_FF1)
                    elif live(g + LAG_FF1 - LAG_PROJ):
                        after(pe, v_ready[m], g + LAG_FF1 - LAG_PROJ)
                    for j in range(2):
                        mm = passes(ps_work[m % 2][:, j * toks:(j + 1) * toks], [
                            (lambda part, kb=kb: w1_s[:, part, kb, (2 * m + j) * P:(2 * m + j + 1) * P],
                             lambda part, kb=kb: x1T[:, part, kb, :]) for kb in range(kd)])
                    mm.then_inc(up_done[m], 1)

            def transpose_x1(g, parity):
                for b in range(PAIR):
                    after(pe, x1_ready[b], g)
                for i in transpose_rows(x1[:, parity], x1T_done):
                    if live(g - LAG_FF1 + LAG_ATTN):
                        after(pe, silu_ready[fc // 2 - 2 + i], g - LAG_FF1 + LAG_ATTN)
                    else:
                        after(pe, xT_lo[i], g + LAG_ATTN)

            def slot_program(t, parity):
                g_proj, g_attn, g_ff1, g_ff2 = t - LAG_PROJ, t - LAG_ATTN, t - LAG_FF1, t - LAG_FF2
                if live(g_attn):
                    scores(g_attn, 0)
                if live(g_ff2):
                    down(g_ff2, 0)
                if live(g_attn):
                    scores(g_attn, 1)
                    transpose_probs(g_attn, 0)
                if live(g_ff2):
                    down(g_ff2, 1)
                if live(g_attn):
                    context(g_attn, 0)
                    transpose_probs(g_attn, 1)
                if live(g_proj):
                    project_qk(g_proj)
                if live(g_attn):
                    output_product(g_attn, 0)
                    context(g_attn, 1)
                if live(g_proj):
                    project_v(g_proj)
                if live(g_attn):
                    output_product(g_attn, 1)
                if live(t):
                    transpose_x(t)
                if live(g_ff1):
                    up(g_ff1)
                if live(g_attn):
                    transpose_x1(g_attn, parity)

            pe.wait_ge(ident_ready, 1)
            pe.wait_ge(pads_zeroed, 1)
            pe.wait_ge(weight_split, n_units)
            run_slots(pe, slot_program)

        @block.scalar
        def _(act):
            act.wait_ge(pads_zeroed, 1)
            for n, (_, at, hi, _, slot) in enumerate(units):
                act.wait_ge(stage_loaded[slot], 16 * (n // STAGE_SLOTS + 1))
                act.activation(hi, at, ACT.Copy).then_inc(weight_hi, 1)
            act.wait_ge(vectors_loaded, 16 * n_vectors)
            act.wait_ge(bq_scaled, 1)

            def exponentials(g, b):
                after(act, max_ready[b], g)
                for head in range(HEADS):
                    e = act.activation(probs[:, b, head, :], probs[:, b, head, :], ACT.Exp,
                                       bias=neg_max[:, b, head:head + 1], accum_out=row_sum[:, b, head:head + 1])
                e.then_inc(exp_ready[b], 1)

            def sum_of_squares(g, b, rows_in, ready, sums, done):
                after(act, ready[b], g)
                act.activation(squares, rows_in, ACT.Square, accum_out=sums[:, b:b + 1]).then_inc(done[b], 1)

            def probsT_out(g, b):
                after(act, probsT_done[b], g)
                act.activation(probs[:, b].rearrange("p h n -> p (h n)"), ps_probsT[:],
                               ACT.Copy).then_inc(probsT_ready[b], 1)

            def context_hi(g, b):
                after(act, ctx_done[b], g)
                act.activation(ctxT[:, HI].rearrange("p c n -> p (c n)"), ps_ctx[:], ACT.Copy).then_inc(ctx_hi[b], 1)

            def queries_out(g):
                for i in range(2):
                    after(act, q_done[i], g)
                    for j in range(2):
                        c = 2 * i + j
                        e = act.activation(q[:, c, :], ps_work[i][:, j * toks:(j + 1) * toks], ACT.Identity,
                                           bias=bq_col[:, c:c + 1], scale=scale)
                    e.then_inc(q_ready[i], 1)

            def transposed_hi(g, done, xT_out, ready):
                for i, blocks in enumerate((2, 1)):
                    after(act, done[i], g)
                    act.activation(xT_out[:, HI, 2 * i:2 * i + blocks, :].rearrange("p c n -> p (c n)"),
                                   ps_work[i][:, 0:blocks * toks], ACT.Copy).then_inc(ready[i], 1)

            def silu(g):
                for m in range(fc // 2):
                    after(act, up_done[m], g)
                    after(act, h_lo[m - 2 if m >= 2 else fc // 2 - 2 + m], g if m >= 2 else g - 1)
                    for j in range(2):
                        e = act.activation(h_raw[:, m % 2, j * toks:(j + 1) * toks],
                                           ps_work[m % 2][:, j * toks:(j + 1) * toks], ACT.Silu,
                                           bias=b1_col[:, 2 * m + j:2 * m + j + 1])
                    e.then_inc(silu_ready[m], 1)

            def slot_program(t, parity):
                g_proj, g_attn, g_ff1, g_ff2 = t - LAG_PROJ, t - LAG_ATTN, t - LAG_FF1, t - LAG_FF2
                if live(g_attn):
                    exponentials(g_attn, 0)
                if live(g_ff2):
                    sum_of_squares(g_ff2, 0, y[:, 0, :], res2_ready, sum_sq2, sq2_ready)
                if live(g_attn):
                    probsT_out(g_attn, 0)
                    exponentials(g_attn, 1)
                if live(g_ff2):
                    sum_of_squares(g_ff2, 1, y[:, 1, :], res2_ready, sum_sq2, sq2_ready)
                if live(g_attn):
                    context_hi(g_attn, 0)
                    probsT_out(g_attn, 1)
                if live(g_proj):
                    queries_out(g_proj)
                if live(g_attn):
                    sum_of_squares(g_attn, 0, x1[:, parity, 0, :], res1_ready, sum_sq1, sq1_ready)
                    context_hi(g_attn, 1)
                    sum_of_squares(g_attn, 1, x1[:, parity, 1, :], res1_ready, sum_sq1, sq1_ready)
                if live(t):
                    transposed_hi(t, xT_done, xT, xT_hi)
                if live(g_ff1):
                    silu(g_ff1)
                if live(g_attn):
                    transposed_hi(g_attn, x1T_done, x1T, x1T_hi)

            run_slots(act, slot_program)

        @block.vector
        def _(dve):
            for n, (_, at, hi, lo, slot) in enumerate(units):
                dve.wait_ge(weight_hi, n + 1)
                dve.tensor_tensor(lo, at, hi.bitcast(F32), ALU.subtract).then_inc(weight_split, 1)
            dve.wait_ge(vectors_loaded, 16 * n_vectors)
            dve.wait_ge(pads_zeroed, 1)
            dve.tensor_scalar(bq_col[:], bq_col[:], scale, None, ALU.mult).then_inc(bq_scaled, 1)

            def bias_and_max(g, b, parity):
                after(dve, scores_done[b], g)
                if b == 0:
                    if static(g):
                        dve.wait_ge(bias_loaded[parity], 16 * (g // 2 + 1))
                    else:
                        dve.wait_ge(bias_loaded[parity], (g - parity) * 8 + 16)
                dve.tensor_tensor(probs[:, b], ps_scores[:].rearrange("p (h n) -> p h n", n=P),
                                  bias[:, parity, b, :].unsqueeze(1).to_broadcast([P, HEADS, P]),
                                  ALU.add).then_inc(scores_biased[b], 1)
                after(dve, scores_biased[b], g)
                dve.tensor_reduce(neg_max[:, b, :], probs[:, b], AX.X, ALU.max,
                                  negate=True).then_inc(max_ready[b], 1)

            def normalise(g, b):
                after(dve, exp_ready[b], g)
                dve.reciprocal(row_inv[:, b, :], row_sum[:, b, :]).then_inc(inv_ready[b], 1)
                after(dve, inv_ready[b], g)
                dve.tensor_tensor(probs[:, b], probs[:, b],
                                  row_inv[:, b, :].unsqueeze(2).to_broadcast([P, HEADS, P]),
                                  ALU.mult).then_inc(probs_ready[b], 1)

            def context_lo(g, b):
                after(dve, ctx_hi[b], g)
                dve.tensor_tensor(ctxT[:, LO].rearrange("p c n -> p (c n)"), ps_ctx[:],
                                  ctxT[:, HI].rearrange("p c n -> p (c n)").bitcast(F32),
                                  ALU.subtract).then_inc(ctx_lo[b], 1)

            def keys_out(g):
                for i in range(2):
                    after(dve, k_done[i], g)
                    for j in range(2):
                        c = 2 * i + j
                        e = dve.tensor_scalar(k[:, c, :], ps_work[i][:, j * toks:(j + 1) * toks],
                                              bk_col[:, c:c + 1], None, ALU.add)
                    e.then_inc(k_ready[i], 1)

            def values_out(g):
                for b in range(PAIR):
                    after(dve, v_done[b], g)
                    dve.tensor_tensor(v[:, b, :, 0:dh], ps_work[b][:, 0:d].rearrange("p (h e) -> p h e", e=dh),
                                      rows[:, BV, :].rearrange("p (h e) -> p h e", e=dh),
                                      ALU.add).then_inc(v_ready[b], 1)

            def transposed_lo(g, hi_ready, xT_out, ready):
                for i, blocks in enumerate((2, 1)):
                    after(dve, hi_ready[i], g)
                    part = [xT_out[:, p, 2 * i:2 * i + blocks, :].rearrange("p c n -> p (c n)") for p in (HI, LO)]
                    dve.tensor_tensor(part[LO], ps_work[i][:, 0:blocks * toks], part[HI].bitcast(F32),
                                      ALU.subtract).then_inc(ready[i], 1)

            def residual1(g, b, parity):
                if b == 0:
                    after(dve, x_res_biased, g)
                after(dve, attn_done[b], g)
                dve.tensor_tensor(x1[:, parity, b, :], ps_rows[:, 0:d], x_res[:, b, :],
                                  ALU.add).then_inc(res1_ready[b], 1)

            def norm1(g, b, parity):
                after(dve, rms1_ready[b], g)
                dve.scalar_tensor_tensor(out=x1[:, parity, b, :], in0=x1[:, parity, b, :],
                                         scalar=inv_rms1[:, b:b + 1], in1=rows[:, ALPHA1, :],
                                         op0=ALU.mult, op1=ALU.mult).then_inc(x1_scaled[b], 1)
                after(dve, x1_scaled[b], g)
                dve.tensor_tensor(x1[:, parity, b, :], x1[:, parity, b, :], rows[:, GAMMA1, :],
                                  ALU.add).then_inc(x1_ready[b], 1)

            def split_h(g, m):
                hi = h[:, HI, 2 * m:2 * m + 2, :].rearrange("p c n -> p (c n)")
                after(dve, silu_ready[m], g)
                dve.tensor_copy(hi, h_raw[:, m % 2, :]).then_inc(h_hi[m], 1)
                after(dve, h_hi[m], g)
                dve.tensor_tensor(h[:, LO, 2 * m:2 * m + 2, :].rearrange("p c n -> p (c n)"), h_raw[:, m % 2, :],
                                  hi.bitcast(F32), ALU.subtract).then_inc(h_lo[m], 1)

            def residual2(g, b, parity):
                if b == 0:
                    after(dve, x1_b2_ready, g)
                    after(dve, y_stored, g - 1, 16)
                after(dve, down_done[b], g)
                dve.tensor_tensor(y[:, b, :], ps_rows[:, 0:d], x1[:, parity, b, :],
                                  ALU.add).then_inc(res2_ready[b], 1)

            def norm2_and_stats(g, b):
                after(dve, rms2_ready[b], g)
                dve.scalar_tensor_tensor(out=y[:, b, :], in0=y[:, b, :], scalar=inv_rms2[:, b:b + 1],
                                         in1=rows[:, ALPHA2, :], op0=ALU.mult,
                                         op1=ALU.mult).then_inc(y_scaled[b], 1)
                after(dve, y_scaled[b], g)
                if b == 0:
                    after(dve, x_last_biased, g)
                dve.tensor_tensor(y[:, b, :], y[:, b, :], x_last[:, b, :], ALU.add).then_inc(y_summed[b], 1)
                after(dve, y_summed[b], g)
                dve.bn_stats(stats[:, b, :], y[:, b, :]).then_inc(stats_ready[b], 1)
                after_apart(dve, stats_ready[b], g)
                dve.bn_aggr(mean_var[:, b, :], stats[:, b, :]).then_inc(var_ready[b], 1)

            def layer_norm(g, b):
                after(dve, std_ready[b], g)
                dve.tensor_scalar(y[:, b, :], y[:, b, :], mean_var[:, b, 0:1], inv_std[:, b:b + 1],
                                  ALU.subtract, ALU.mult).then_inc(y_ready[b], 1)

            def slot_program(t, parity):
                g_proj, g_attn, g_ff1, g_ff2 = t - LAG_PROJ, t - LAG_ATTN, t - LAG_FF1, t - LAG_FF2
                if live(g_attn):
                    bias_and_max(g_attn, 0, parity)
                    normalise(g_attn, 0)
                if live(g_ff2):
                    residual2(g_ff2, 0, parity)
                if live(g_attn):
                    bias_and_max(g_attn, 1, parity)
                if live(g_ff2):
                    norm2_and_stats(g_ff2, 0)
                if live(g_attn):
                    normalise(g_attn, 1)
                if live(g_ff2):
                    layer_norm(g_ff2, 0)
                    residual2(g_ff2, 1, parity)
                if live(g_attn):
                    context_lo(g_attn, 0)
                if live(g_ff2):
                    norm2_and_stats(g_ff2, 1)
                if live(g_proj):
                    keys_out(g_proj)
                if live(g_ff2):
                    layer_norm(g_ff2, 1)
                if live(g_attn):
                    residual1(g_attn, 0, parity)
                    context_lo(g_attn, 1)
                if live(g_proj):
                    values_out(g_proj)
                if live(g_attn):
                    norm1(g_attn, 0, parity)
                    residual1(g_attn, 1, parity)
                if live(t):
                    transposed_lo(t, xT_hi, xT, xT_lo)
                for m in range(fc // 2):
                    if live(g_ff1):
                        split_h(g_ff1, m)
                    if live(g_attn) and m == 1:
                        norm1(g_attn, 1, parity)
                if live(g_attn):
                    transposed_lo(g_attn, x1T_hi, x1T, x1T_lo)

            run_slots(dve, slot_program)


_INS = ["x", "adj"] + ["L0_gnn_" + n for n in (
    "wq", "bq", "wk", "bk", "wv", "bv", "wo", "bo", "w1", "b1", "w2", "b2",
    "alpha1", "gamma1", "alpha2", "gamma2")]


def kernel(**inputs):
    import numpy as _np
    import concourse.bacc as _bacc
    from concourse import mybir as _mybir
    from concourse.bass_utils import run_bass_kernel_spmd as _run

    nc = _bacc.Bacc("TRN2", target_bir_lowering=False, num_devices=1, dynamic_dma_scratch_size=1024)
    arrays, args = {}, []
    for name in _INS:
        a = _np.ascontiguousarray(inputs[name])
        arrays[f"in_{name}"] = a
        args.append(nc.dram_tensor(f"in_{name}", a.shape, _mybir.dt.from_np(a.dtype), kind="ExternalInput").ap())
    args.append(nc.dram_tensor("out", inputs["x"].shape, F32, kind="ExternalOutput").ap())
    build_layer(nc, *args)
    r = _run(nc, [arrays], core_ids=[0])
    return r.results[0]["out"]
```

```python
from contextlib import ExitStack

import concourse.bass as bass
from concourse import mybir

F32 = mybir.dt.float32
F32R = mybir.dt.float32r
ALU = mybir.AluOpType
ACT = mybir.ActivationFunctionType
AX = mybir.AxisListType

P = 128
PAIR = 2
HEADS = 8
HALF = 64
TILE = 32
HI, LO = 0, 1
PASSES = ((LO, HI), (HI, LO), (HI, HI))
RMS_EPS = 1e-6
LN_EPS = 1e-5
STAGE_SLOTS = 6
UNROLL = 4
LAG_PROJ, LAG_ATTN, LAG_FF1, LAG_FF2 = 1, 2, 3, 4


def build_layer(nc, x, adj, wq, bq, wk, bk, wv, bv, wo, bo, w1, b1, w2, b2,
                alpha1, gamma1, alpha2, gamma2, out):
    graphs, nodes, d = x.shape
    f = w1.shape[1]
    rest = d // HEADS - TILE
    groups = graphs // PAIR
    toks = PAIR * nodes
    dh = d // HEADS
    kd = d // P
    hp = HEADS // 2
    fc = f // P
    scale = float(dh) ** -0.5
    slots = groups + LAG_FF2
    loop_from, loop_to = -(-(LAG_FF2 + 2) // UNROLL) * UNROLL, groups
    assert nodes == P and kd * P == d and HEADS == 8 and 2 * rest == TILE and dh <= HALF
    assert UNROLL % 2 == 0 and loop_to % UNROLL == 0

    ctx = ExitStack()
    with ctx:
        def sb(name, shape, dt=F32):
            return ctx.enter_context(nc.sbuf_tensor(name, shape, dt))

        def ps(name, cols):
            return ctx.enter_context(nc.psum_tensor(name, [P, cols], F32))

        def sem(name):
            return ctx.enter_context(nc.semaphore(name))

        def sems(name, n):
            return [sem(f"{name}{i}") for i in range(n)]

        ctx.enter_context(nc.allow_non_contiguous_dma(reason="biases laid out by partition, once"))

        wq_s = sb("wq_s", [P, 2, kd, d], F32R)
        wk_s = sb("wk_s", [P, 2, kd, d], F32R)
        wv_s = sb("wv_s", [P, 2, kd, d], F32R)
        wo_s = sb("wo_s", [P, 2, kd, d], F32R)
        w1_s = sb("w1_s", [P, 2, kd, f], F32R)
        w2_s = sb("w2_s", [P, 2, fc, d], F32R)
        stage = sb("stage", [P, STAGE_SLOTS, d])
        bq_col = sb("bq_col", [P, kd])
        bk_col = sb("bk_col", [P, kd])
        b1_col = sb("b1_col", [P, fc])
        rows = sb("rows", [P, 7, d])
        BO, BV, B2, ALPHA1, GAMMA1, ALPHA2, GAMMA2 = range(7)
        ident = sb("ident", [P, P])
        neg_half = sb("neg_half", [P, 1])
        x_in = sb("x_in", [P, PAIR, d])
        x_res = sb("x_res", [P, PAIR, d])
        x_last = sb("x_last", [P, PAIR, d])
        bias = sb("bias", [P, 2, PAIR, P])
        xT = sb("xT", [P, 2, kd, toks], F32R)
        Q, K = 0, 1
        qk_flat = sb("qk_flat", [P, 2, kd, toks])
        qk = sb("qk", [P, 2, hp, toks])
        v_first = sb("v_first", [P, PAIR, HEADS, TILE])
        v_rest = sb("v_rest", [P, PAIR, HEADS, TILE])
        probs = sb("probs", [P, PAIR, HEADS, P])
        neg_max = sb("neg_max", [P, PAIR, HEADS])
        row_sum = sb("row_sum", [P, PAIR, HEADS])
        row_inv = sb("row_inv", [P, PAIR, HEADS])
        ctxT = sb("ctxT", [P, 2, kd, P], F32R)
        x1 = sb("x1", [P, 2, PAIR, d])
        x1T = sb("x1T", [P, 2, kd, toks], F32R)
        h_raw = sb("h_raw", [P, 2, 2 * toks])
        h = sb("h", [P, 2, fc, toks], F32R)
        y = sb("y", [P, PAIR, d])
        squares = sb("squares", [P, d])
        sum_sq1 = sb("sum_sq1", [P, PAIR])
        sum_sq2 = sb("sum_sq2", [P, PAIR])
        mean_sq1 = sb("mean_sq1", [P, PAIR])
        mean_sq2 = sb("mean_sq2", [P, PAIR])
        inv_rms1 = sb("inv_rms1", [P, PAIR])
        inv_rms2 = sb("inv_rms2", [P, PAIR])
        stats = sb("stats", [P, PAIR, 6])
        mean_var = sb("mean_var", [P, PAIR, 2])
        var_eps = sb("var_eps", [P, PAIR])
        inv_std = sb("inv_std", [P, PAIR])

        ps_scores = ps("ps_scores", HEADS * P)
        ps_probsT = ps("ps_probsT", HEADS * P)
        ps_ctx = ps("ps_ctx", 512)
        ps_rows = ps("ps_rows", 512)
        ps_work = [ps("ps_work0", 512), ps("ps_work1", 512)]

        stage_loaded = sems("stage_loaded", STAGE_SLOTS)
        weight_hi = sem("weight_hi")
        weight_split = sem("weight_split")
        vectors_loaded = sem("vectors_loaded")
        pads_zeroed = sem("pads_zeroed")
        bq_scaled = sem("bq_scaled")
        ident_zeroed = sem("ident_zeroed")
        ident_ready = sem("ident_ready")
        x_in_loaded = sem("x_in_loaded")
        x_res_loaded = sem("x_res_loaded")
        x_last_loaded = sem("x_last_loaded")
        bias_loaded = sems("bias_loaded", 2)
        y_stored = sem("y_stored")
        xT_done = sems("xT_done", 2)
        xT_hi = sems("xT_hi", 2)
        xT_lo = sems("xT_lo", 2)
        qk_done, qk_ready = sems("qk_done", 3), sems("qk_ready", 3)
        qk_moved = sem("qk_moved")
        v_done, v_ready = sems("v_done", PAIR), sems("v_ready", PAIR)
        scores_done = sems("scores_done", PAIR)
        scores_biased = sems("scores_biased", PAIR)
        max_ready = sems("max_ready", PAIR)
        exp_ready = sems("exp_ready", PAIR)
        inv_ready = sems("inv_ready", PAIR)
        probs_ready = sems("probs_ready", PAIR)
        probsT_done = sems("probsT_done", PAIR)
        probsT_ready = sems("probsT_ready", PAIR)
        ctx_done = sems("ctx_done", PAIR)
        ctx_hi = sems("ctx_hi", PAIR)
        ctx_lo = sems("ctx_lo", PAIR)
        attn_done = sems("attn_done", PAIR)
        x_res_biased = sem("x_res_biased")
        res1_ready = sems("res1_ready", PAIR)
        sq1_ready = sems("sq1_ready", PAIR)
        ms1_ready = sems("ms1_ready", PAIR)
        rms1_ready = sems("rms1_ready", PAIR)
        x1_scaled = sems("x1_scaled", PAIR)
        x1_ready = sems("x1_ready", PAIR)
        x1_b2_ready = sem("x1_b2_ready")
        x1T_done = sems("x1T_done", 2)
        x1T_hi = sems("x1T_hi", 2)
        x1T_lo = sems("x1T_lo", 2)
        up_done = sems("up_done", fc // 2)
        silu_ready = sems("silu_ready", fc // 2)
        h_hi = sems("h_hi", fc // 2)
        h_lo = sems("h_lo", fc // 2)
        down_done = sems("down_done", PAIR)
        x_last_biased = sem("x_last_biased")
        res2_ready = sems("res2_ready", PAIR)
        sq2_ready = sems("sq2_ready", PAIR)
        ms2_ready = sems("ms2_ready", PAIR)
        rms2_ready = sems("rms2_ready", PAIR)
        y_scaled = sems("y_scaled", PAIR)
        y_summed = sems("y_summed", PAIR)
        stats_ready = sems("stats_ready", PAIR)
        var_ready = sems("var_ready", PAIR)
        var_eps_ready = sems("var_eps_ready", PAIR)
        std_ready = sems("std_ready", PAIR)
        y_ready = sems("y_ready", PAIR)

        def static(g):
            return isinstance(g, int)

        units = []
        loads_of_slot = [0] * STAGE_SLOTS

        def unit(loads, parts):
            slot = len(units) % STAGE_SLOTS
            loads_of_slot[slot] += len(loads)
            units.append((loads, parts[HI], parts[LO], 16 * loads_of_slot[slot]))

        for w_dram, w_sb in ((wq, wq_s), (wk, wk_s), (wv, wv_s)):
            for kb in range(kd):
                unit([(0, P, w_dram[kb * P:(kb + 1) * P, :])], [w_sb[:, part, kb, :] for part in (HI, LO)])
        proj_units = len(units)
        wo_rows = wo.rearrange("(h e) n -> h e n", e=dh)
        for c in range(2):
            unit([(j * TILE, TILE, wo_rows[4 * c + j, 0:TILE, :]) for j in range(4)],
                 [wo_s[:, part, c, :] for part in (HI, LO)])
        unit([(j * rest, rest, wo_rows[j, TILE:dh, :]) for j in range(HEADS)],
             [wo_s[:, part, 2, :] for part in (HI, LO)])
        out_units = len(units)
        for kb in range(kd):
            for n in range(0, f, d):
                unit([(0, P, w1[kb * P:(kb + 1) * P, n:n + d])], [w1_s[:, part, kb, n:n + d] for part in (HI, LO)])
        up_units = len(units)
        for m in range(fc):
            unit([(0, P, w2[m * P:(m + 1) * P, :])], [w2_s[:, part, m, :] for part in (HI, LO)])

        schedule = {(0, 5): range(proj_units), (2, 0): range(proj_units, out_units)}
        for t_split, first, of_point in ((2, out_units, (0, 2, 3, 4, 3, 0)), (3, up_units, (2, 2, 2, 2, 2, 2))):
            for point, pieces in enumerate(of_point):
                if pieces:
                    schedule[t_split, point] = range(first, first + pieces)
                first += pieces

        def weights_due(t, point):
            return schedule.get((t, point), ()) if static(t) else ()

        n_vectors = 10

        moves = []
        for head in range(HEADS):
            at = 0
            while at < dh:
                c, p0 = divmod(head * dh + at, P)
                n = min(dh - at, P - p0)
                moves.append((p0, c, head % 2 * HALF + at, head // 2, n))
                at += n

        def place(head):
            return head % 2 * hp + head // 2

        def live(g):
            return not static(g) or 0 <= g < groups

        def through(g, each=1):
            return (g + 1) * each

        def run_slots(engine, slot):
            for t in range(loop_from):
                slot(t, t % 2)
            with engine.Fori(loop_from // UNROLL, loop_to // UNROLL) as turn:
                for i in range(UNROLL):
                    slot(turn * UNROLL + i, i % 2)
            for t in range(loop_to, slots):
                slot(t, t % 2)

        def group_rows(ap, g):
            if static(g):
                return ap[g * PAIR:(g + 1) * PAIR].rearrange("b n e -> n b e")
            return ap[bass.ds(g * PAIR, PAIR)].rearrange("b n e -> n b e")

        block = ctx.enter_context(nc.Block())

        @block.sync
        def _(sp):
            def load_x(g):
                for i in range(2):
                    if live(g - 1):
                        sp.wait_ge(xT_done[i], through(g - 1))
                sp.dma_start(x_in[:], group_rows(x, g)).then_inc(x_in_loaded, 16)

            def load_weights(n):
                slot = n % STAGE_SLOTS
                if n >= STAGE_SLOTS:
                    sp.wait_ge(weight_split, n - STAGE_SLOTS + 1)
                for p0, rows_n, src in units[n][0]:
                    sp.dma_start(stage[p0:p0 + rows_n, slot, :], src).then_inc(stage_loaded[slot], 16)

            load_x(0)
            for n in range(STAGE_SLOTS):
                load_weights(n)
            for col, src in ((bq_col, bq), (bk_col, bk), (b1_col, b1)):
                sp.dma_start(col[:], src.rearrange("(c p) -> p c", p=P)).then_inc(vectors_loaded, 16)
            for i, row in enumerate((bo, bv, b2, alpha1, gamma1, alpha2, gamma2)):
                sp.dma_start(rows[:, i, :], row.partition_broadcast(P)).then_inc(vectors_loaded, 16)

            def slot_program(t, parity):
                if live(t) and not (static(t) and t == 0):
                    load_x(t)
                g = t - LAG_ATTN
                if live(g):
                    for b in range(PAIR):
                        if live(g - 1):
                            sp.wait_ge(res1_ready[b], through(g - 1))
                    sp.dma_start(x_res[:], group_rows(x, g)).then_inc(x_res_loaded, 16)
                g = t - LAG_PROJ
                if live(g):
                    if live(g - 2):
                        sp.wait_ge(scores_biased[PAIR - 1], through(g - 2))
                    sp.dma_start(bias[:, 1 - parity],
                                 group_rows(adj, g)).then_inc(bias_loaded[1 - parity], 16)
                for point in range(1, 6):
                    for n in weights_due(t, point):
                        if n >= STAGE_SLOTS:
                            load_weights(n)
                g = t - LAG_FF1
                if live(g):
                    for b in range(PAIR):
                        if live(g - 1):
                            sp.wait_ge(y_summed[b], through(g - 1))
                    sp.dma_start(x_last[:], group_rows(x, g)).then_inc(x_last_loaded, 16)
                g = t - LAG_FF2
                if live(g):
                    for b in range(PAIR):
                        sp.wait_ge(y_ready[b], through(g))
                    sp.dma_start(group_rows(out, g), y[:]).then_inc(y_stored, 16)
                g = t - LAG_PROJ
                if live(g):
                    for i in range(3):
                        sp.wait_ge(qk_ready[i], through(g))
                    for p0, c, to, pair, n in moves:
                        sp.dma_start(qk[to:to + n, :, pair, :], qk_flat[p0:p0 + n, :, c, :]).then_inc(qk_moved, 16)
                if static(t):
                    for n in weights_due(t + 1, 0):
                        load_weights(n)

            run_slots(sp, slot_program)
            sp.wait_ge(y_stored, 16 * groups)

        @block.gpsimd
        def _(pool):
            pool.memset(v_rest[:], 0.0)
            pool.memset(neg_half[:], -0.5).then_inc(pads_zeroed, 1)
            pool.memset(ident[:], 0.0).then_inc(ident_zeroed, 1)
            pool.wait_ge(ident_zeroed, 1)
            pool.affine_select(out=ident[:], in_=ident[:], compare_op=ALU.not_equal, fill=1.0, base=0,
                               pattern=[[-1, P]], channel_multiplier=1).then_inc(ident_ready, 1)
            pool.wait_ge(vectors_loaded, 16 * n_vectors)
            pool.wait_ge(pads_zeroed, 1)

            def row(i):
                return rows[:, i, :].unsqueeze(1).to_broadcast([P, PAIR, d])

            def inverse_root(b, source, s_source, g, times, eps, shifted, s_shifted, result, s_result):
                pool.wait_ge(vectors_loaded, 16 * n_vectors)
                pool.wait_ge(s_source[b], through(g))
                pool.tensor_scalar(shifted[:, b:b + 1], source, times, eps, ALU.mult,
                                   ALU.add).then_inc(s_shifted[b], 1)
                pool.wait_ge(s_shifted[b], through(g))
                pool.tensor_tensor(result[:, b:b + 1], shifted[:, b:b + 1], neg_half[:],
                                   ALU.pow).then_inc(s_result[b], 1)

            def slot_program(t, parity):
                g_ff2 = t - LAG_FF2
                g_attn = t - LAG_ATTN
                if live(g_ff2):
                    pool.wait_ge(x_last_loaded, through(g_ff2, 16))
                    pool.tensor_tensor(x_last[:], x_last[:], row(GAMMA2),
                                       ALU.add).then_inc(x_last_biased, 1)
                if live(g_attn):
                    pool.wait_ge(x_res_loaded, through(g_attn, 16))
                    pool.tensor_tensor(x_res[:], x_res[:], row(BO), ALU.add).then_inc(x_res_biased, 1)
                if live(g_ff2):
                    for b in range(PAIR):
                        inverse_root(b, sum_sq2[:, b:b + 1], sq2_ready, g_ff2, 1.0 / d, RMS_EPS,
                                     mean_sq2, ms2_ready, inv_rms2, rms2_ready)
                        inverse_root(b, mean_var[:, b, 1:2], var_ready, g_ff2, 1.0, LN_EPS,
                                     var_eps, var_eps_ready, inv_std, std_ready)
                if live(g_attn):
                    for b in range(PAIR):
                        inverse_root(b, sum_sq1[:, b:b + 1], sq1_ready, g_attn, 1.0 / d, RMS_EPS,
                                     mean_sq1, ms1_ready, inv_rms1, rms1_ready)
                    for i in range(2):
                        pool.wait_ge(x1T_done[i], through(g_attn))
                    pool.tensor_tensor(x1[:, parity], x1[:, parity], row(B2),
                                       ALU.add).then_inc(x1_b2_ready, 1)

            run_slots(pool, slot_program)

        @block.tensor
        def _(pe):
            def passes(ps_out, pairs):
                n = len(PASSES) * len(pairs)
                i = 0
                for stationary, moving in pairs:
                    for sta, mov in PASSES:
                        mm = pe.matmul(ps_out, stationary(sta), moving(mov), start=(i == 0), stop=(i == n - 1))
                        i += 1
                return mm

            def scores(g, b):
                if b == 0:
                    pe.wait_ge(qk_moved, through(g, 16 * len(moves)))
                    if live(g - 1):
                        pe.wait_ge(scores_biased[PAIR - 1], through(g - 1))
                else:
                    pe.wait_ge(scores_biased[b - 1], through(g))
                for head in range(HEADS):
                    c, p0 = head // 2, head % 2 * HALF
                    at = place(head) * P
                    mm = pe.matmul(ps_scores[:, at:at + P],
                                   qk[p0:p0 + dh, Q, c, b * P:(b + 1) * P],
                                   qk[p0:p0 + dh, K, c, b * P:(b + 1) * P],
                                   start=True, stop=True)
                mm.then_inc(scores_done[b], 1)

            def transpose_probs(g, b):
                pe.wait_ge(probs_ready[b], through(g, 2))
                if b:
                    pe.wait_ge(probsT_ready[b - 1], through(g))
                else:
                    if live(g - 1):
                        pe.wait_ge(probsT_ready[PAIR - 1], through(g - 1))
                for head in range(HEADS):
                    mm = pe.transpose(ps_probsT[:, head * P:(head + 1) * P], probs[:, b, head, :], ident[:])
                mm.then_inc(probsT_done[b], 1)

            def context(g, b):
                pe.wait_ge(probsT_ready[b], through(g))
                pe.wait_ge(v_ready[b], through(g))
                if b:
                    pe.wait_ge(ctx_lo[b - 1], through(g))
                else:
                    if live(g - 1):
                        pe.wait_ge(x1T_lo[1], through(g - 1))
                    if live(g + LAG_ATTN - 1):
                        pe.wait_ge(xT_lo[1], through(g + LAG_ATTN - 1))
                for side in range(2):
                    for pair in range(hp):
                        head = 2 * pair + side
                        pe.matmul(ps_ctx[pair * TILE:(pair + 1) * TILE, 2 * P:3 * P], v_rest[:, b, head, :],
                                  probs[:, b, place(head), :], start=(side == 0), stop=(side == 1))
                for head in range(HEADS):
                    p0, at = head % 4 * TILE, head // 4 * P
                    mm = pe.matmul(ps_ctx[p0:p0 + TILE, at:at + P], v_first[:, b, head, :],
                                   probs[:, b, place(head), :], start=True, stop=True)
                mm.then_inc(ctx_done[b], 1)

            def output_product(g, b):
                pe.wait_ge(ctx_lo[b], through(g))
                if b:
                    pe.wait_ge(res1_ready[b - 1], through(g))
                elif live(g - LAG_FF2 + LAG_ATTN):
                    pe.wait_ge(res2_ready[PAIR - 1], through(g - LAG_FF2 + LAG_ATTN))
                else:
                    if live(g - 1):
                        pe.wait_ge(res1_ready[PAIR - 1], through(g - 1))
                passes(ps_rows[:, 0:d], [
                    (lambda part, c=c: ctxT[:, part, c, :], lambda part, c=c: wo_s[:, part, c, :])
                    for c in range(kd)]).then_inc(attn_done[b], 1)

            def down(g, b):
                if b == 0:
                    if live(g + LAG_FF2 - LAG_ATTN - 1):
                        pe.wait_ge(res1_ready[PAIR - 1], through(g + LAG_FF2 - LAG_ATTN - 1))
                    else:
                        if live(g - 1):
                            pe.wait_ge(res2_ready[PAIR - 1], through(g - 1))
                else:
                    pe.wait_ge(res2_ready[b - 1], through(g))
                for m in range(fc):
                    if b == 0 and m % 2 == 0:
                        pe.wait_ge(h_lo[m // 2], through(g))
                    for i, (sta, mov) in enumerate(PASSES):
                        mm = pe.matmul(ps_rows[:, 0:d], h[:, sta, m, b * P:(b + 1) * P], w2_s[:, mov, m, :],
                                       start=(m == 0 and i == 0), stop=(m == fc - 1 and i == len(PASSES) - 1))
                mm.then_inc(down_done[b], 1)

            def project_qk(g):
                for i in range(2):
                    pe.wait_ge(xT_lo[i], through(g))
                for n, blocks in enumerate((((wq_s, 0), (wq_s, 1)), ((wq_s, 2), (wk_s, 0)),
                                            ((wk_s, 1), (wk_s, 2)))):
                    if static(g) and g == 0 and n < 2:
                        pe.wait_ge(weight_split, (n + 1) * kd)
                    if n == 0:
                        if live(g - LAG_ATTN + LAG_PROJ - 1):
                            pe.wait_ge(x1T_lo[0], through(g - LAG_ATTN + LAG_PROJ - 1))
                    elif n == 1 and live(g - LAG_FF1 + LAG_PROJ - 1):
                        pe.wait_ge(silu_ready[fc // 2 - 1], through(g - LAG_FF1 + LAG_PROJ - 1))
                    elif n == 2:
                        pe.wait_ge(qk_ready[0], through(g))
                    for j, (w, c) in enumerate(blocks):
                        mm = passes(ps_work[n % 2][:, j * toks:(j + 1) * toks], [
                            (lambda part, kb=kb: w[:, part, kb, c * P:(c + 1) * P],
                             lambda part, kb=kb: xT[:, part, kb, :]) for kb in range(kd)])
                    mm.then_inc(qk_done[n], 1)

            def project_v(g):
                if static(g) and g == 0:
                    pe.wait_ge(weight_split, proj_units)
                for b in range(PAIR):
                    pe.wait_ge(qk_ready[b + 1], through(g))
                    passes(ps_work[1 - b][:, 0:d], [
                        (lambda part, kb=kb: xT[:, part, kb, b * P:(b + 1) * P],
                         lambda part, kb=kb: wv_s[:, part, kb, :]) for kb in range(kd)]).then_inc(v_done[b], 1)

            def transpose_rows(ps_out, rows_in, blocks, done):
                for kb in blocks:
                    for b in range(PAIR):
                        at = kb % 2 * toks + b * P
                        mm = pe.transpose(ps_out[:, at:at + P], rows_in[:, b, kb * P:(kb + 1) * P], ident[:])
                mm.then_inc(done, 1)

            def transpose_x(g, i):
                if i == 0:
                    pe.wait_ge(x_in_loaded, through(g, 16))
                    if live(g - LAG_PROJ):
                        pe.wait_ge(v_ready[0], through(g - LAG_PROJ))
                    transpose_rows(ps_work[1], x_in, (0, 1), xT_done[0])
                else:
                    if live(g - LAG_ATTN):
                        pe.wait_ge(ctx_lo[PAIR - 1], through(g - LAG_ATTN))
                    transpose_rows(ps_ctx, x_in, (2,), xT_done[1])

            def up(g):
                for i in range(2):
                    pe.wait_ge(x1T_lo[i], through(g))
                for m in range(fc // 2):
                    if m >= 2:
                        pe.wait_ge(silu_ready[m - 2], through(g))
                    elif m == 0 and live(g + LAG_FF1 - LAG_PROJ):
                        pe.wait_ge(v_ready[1], through(g + LAG_FF1 - LAG_PROJ))
                    elif m == 1 and live(g + LAG_FF1):
                        pe.wait_ge(xT_lo[0], through(g + LAG_FF1))
                    elif m == 1 and live(g + LAG_FF1 - LAG_PROJ):
                        pe.wait_ge(v_ready[0], through(g + LAG_FF1 - LAG_PROJ))
                    for j in range(2):
                        mm = passes(ps_work[m % 2][:, j * toks:(j + 1) * toks], [
                            (lambda part, kb=kb: w1_s[:, part, kb, (2 * m + j) * P:(2 * m + j + 1) * P],
                             lambda part, kb=kb: x1T[:, part, kb, :]) for kb in range(kd)])
                    mm.then_inc(up_done[m], 1)

            def transpose_x1(g, parity):
                for b in range(PAIR):
                    pe.wait_ge(x1_ready[b], through(g))
                if live(g - LAG_FF1 + LAG_ATTN):
                    pe.wait_ge(silu_ready[fc // 2 - 2], through(g - LAG_FF1 + LAG_ATTN))
                else:
                    if live(g - LAG_PROJ + LAG_ATTN):
                        pe.wait_ge(v_ready[1], through(g - LAG_PROJ + LAG_ATTN))
                transpose_rows(ps_work[0], x1[:, parity], (0, 1), x1T_done[0])
                if live(g + LAG_ATTN):
                    pe.wait_ge(xT_lo[1], through(g + LAG_ATTN))
                else:
                    pe.wait_ge(ctx_lo[PAIR - 1], through(g))
                transpose_rows(ps_ctx, x1[:, parity], (2,), x1T_done[1])

            def slot_program(t, parity):
                g_proj, g_attn, g_ff1, g_ff2 = t - LAG_PROJ, t - LAG_ATTN, t - LAG_FF1, t - LAG_FF2
                if live(g_attn):
                    scores(g_attn, 0)
                if live(g_ff2):
                    if static(t) and t == LAG_FF2:
                        pe.wait_ge(weight_split, len(units))
                    down(g_ff2, 0)
                if live(g_attn):
                    scores(g_attn, 1)
                    transpose_probs(g_attn, 0)
                if live(g_ff2):
                    down(g_ff2, 1)
                if live(g_attn):
                    context(g_attn, 0)
                    transpose_probs(g_attn, 1)
                if live(g_proj):
                    project_qk(g_proj)
                if live(g_attn):
                    if static(t) and t == LAG_ATTN:
                        pe.wait_ge(weight_split, out_units)
                    output_product(g_attn, 0)
                    context(g_attn, 1)
                if live(g_proj):
                    project_v(g_proj)
                if live(t):
                    transpose_x(t, 0)
                if live(g_attn):
                    output_product(g_attn, 1)
                if live(t):
                    transpose_x(t, 1)
                if live(g_ff1):
                    if static(t) and t == LAG_FF1:
                        pe.wait_ge(weight_split, up_units)
                    up(g_ff1)
                if live(g_attn):
                    transpose_x1(g_attn, parity)

            pe.wait_ge(ident_ready, 1)
            pe.wait_ge(pads_zeroed, 1)
            run_slots(pe, slot_program)

        @block.scalar
        def _(act):
            def weights_hi(t, point):
                for n in weights_due(t, point):
                    _, hi, _, loaded = units[n]
                    act.wait_ge(stage_loaded[n % STAGE_SLOTS], loaded)
                    act.activation(hi, stage[:, n % STAGE_SLOTS, :], ACT.Copy).then_inc(weight_hi, 1)

            def exponentials(g, b):
                act.wait_ge(max_ready[b], through(g))
                for head in range(HEADS):
                    e = act.activation(probs[:, b, head, :], probs[:, b, head, :], ACT.Exp,
                                       bias=neg_max[:, b, head:head + 1], accum_out=row_sum[:, b, head:head + 1])
                    if head % hp == hp - 1:
                        e.then_inc(exp_ready[b], 1)

            def sum_of_squares(g, b, rows_in, ready, sums, done):
                act.wait_ge(ready[b], through(g))
                act.activation(squares[:], rows_in, ACT.Square, accum_out=sums[:, b:b + 1]).then_inc(done[b], 1)

            def probsT_out(g, b):
                act.wait_ge(probsT_done[b], through(g))
                act.activation(probs[:, b].rearrange("p h n -> p (h n)"), ps_probsT[:],
                               ACT.Copy).then_inc(probsT_ready[b], 1)

            def context_hi(g, b):
                act.wait_ge(ctx_done[b], through(g))
                act.activation(ctxT[:, HI].rearrange("p c n -> p (c n)"), ps_ctx[:, 0:d],
                               ACT.Copy).then_inc(ctx_hi[b], 1)

            def queries_out(g):
                for n, blocks in enumerate(((0, 1), (2,))):
                    act.wait_ge(qk_done[n], through(g))
                    if n == 0:
                        if live(g - 1):
                            act.wait_ge(qk_moved, through(g - 1, 16 * len(moves)))
                    for j, c in enumerate(blocks):
                        e = act.activation(qk_flat[:, Q, c, :], ps_work[n][:, j * toks:(j + 1) * toks], ACT.Identity,
                                           bias=bq_col[:, c:c + 1], scale=scale)
                    if n == 1:
                        e = act.activation(qk_flat[:, K, 0, :], ps_work[1][:, toks:2 * toks], ACT.Identity,
                                           bias=bk_col[:, 0:1])
                    e.then_inc(qk_ready[n], 1)

            def transposed_hi(g, i, ps_in, done, xT_out, ready):
                blocks = 2 - i
                act.wait_ge(done[i], through(g))
                act.activation(xT_out[:, HI, 2 * i:2 * i + blocks, :].rearrange("p c n -> p (c n)"),
                               ps_in[:, 0:blocks * toks], ACT.Copy).then_inc(ready[i], 1)

            def silu(g):
                for m in range(fc // 2):
                    act.wait_ge(up_done[m], through(g))
                    if m >= 2:
                        act.wait_ge(h_lo[m - 2], through(g))
                    else:
                        if live(g - 1):
                            act.wait_ge(h_lo[fc // 2 - 2 + m], through(g - 1))
                    for j in range(2):
                        e = act.activation(h_raw[:, m % 2, j * toks:(j + 1) * toks],
                                           ps_work[m % 2][:, j * toks:(j + 1) * toks], ACT.Silu,
                                           bias=b1_col[:, 2 * m + j:2 * m + j + 1])
                    e.then_inc(silu_ready[m], 1)

            def slot_program(t, parity):
                g_proj, g_attn, g_ff1, g_ff2 = t - LAG_PROJ, t - LAG_ATTN, t - LAG_FF1, t - LAG_FF2
                if static(t) and t == 1:
                    act.wait_ge(vectors_loaded, 16 * n_vectors)
                    act.wait_ge(bq_scaled, 1)
                if live(g_attn):
                    exponentials(g_attn, 0)
                    weights_hi(t, 0)
                if live(g_ff2):
                    sum_of_squares(g_ff2, 0, y[:, 0, :], res2_ready, sum_sq2, sq2_ready)
                if live(g_attn):
                    probsT_out(g_attn, 0)
                    exponentials(g_attn, 1)
                    act.preload_act_table(ACT.Silu)
                    weights_hi(t, 1)
                if live(g_ff2):
                    sum_of_squares(g_ff2, 1, y[:, 1, :], res2_ready, sum_sq2, sq2_ready)
                if live(g_attn):
                    context_hi(g_attn, 0)
                    probsT_out(g_attn, 1)
                    weights_hi(t, 2)
                if live(g_proj):
                    queries_out(g_proj)
                if live(g_attn):
                    sum_of_squares(g_attn, 0, x1[:, parity, 0, :], res1_ready, sum_sq1, sq1_ready)
                    context_hi(g_attn, 1)
                    weights_hi(t, 3)
                if live(t):
                    transposed_hi(t, 0, ps_work[1], xT_done, xT, xT_hi)
                if live(g_attn):
                    sum_of_squares(g_attn, 1, x1[:, parity, 1, :], res1_ready, sum_sq1, sq1_ready)
                    weights_hi(t, 4)
                if live(t):
                    transposed_hi(t, 1, ps_ctx, xT_done, xT, xT_hi)
                weights_hi(t, 5)
                if live(g_ff1):
                    silu(g_ff1)
                if live(g_attn):
                    transposed_hi(g_attn, 0, ps_work[0], x1T_done, x1T, x1T_hi)
                    transposed_hi(g_attn, 1, ps_ctx, x1T_done, x1T, x1T_hi)
                    act.preload_act_table(ACT.Exp)

            run_slots(act, slot_program)

        @block.vector
        def _(dve):
            dve.wait_ge(pads_zeroed, 1)

            def scale_query_bias():
                dve.wait_ge(vectors_loaded, 16 * n_vectors)
                dve.tensor_scalar(bq_col[:], bq_col[:], scale, None, ALU.mult).then_inc(bq_scaled, 1)

            def weights_lo(t, point):
                for n in weights_due(t, point):
                    _, hi, lo, _ = units[n]
                    dve.wait_ge(weight_hi, n + 1)
                    dve.tensor_tensor(lo, stage[:, n % STAGE_SLOTS, :], hi.bitcast(F32),
                                      ALU.subtract).then_inc(weight_split, 1)

            def bias_and_max(g, b, parity):
                dve.wait_ge(scores_done[b], through(g))
                if b == 0:
                    if static(g):
                        dve.wait_ge(bias_loaded[parity], 16 * (g // 2 + 1))
                    else:
                        dve.wait_ge(bias_loaded[parity], (g - parity) * 8 + 16)
                dve.tensor_tensor(probs[:, b], ps_scores[:].rearrange("p (h n) -> p h n", n=P),
                                  bias[:, parity, b, :].unsqueeze(1).to_broadcast([P, HEADS, P]),
                                  ALU.add).then_inc(scores_biased[b], 1)
                dve.wait_ge(scores_biased[b], through(g))
                dve.tensor_reduce(neg_max[:, b, :], probs[:, b], AX.X, ALU.max,
                                  negate=True).then_inc(max_ready[b], 1)

            def normalise(g, b):
                for half in range(2):
                    heads = slice(half * hp, (half + 1) * hp)
                    dve.wait_ge(exp_ready[b], through(g, 2) - 1 + half)
                    dve.reciprocal(row_inv[:, b, heads], row_sum[:, b, heads]).then_inc(inv_ready[b], 1)
                    dve.wait_ge(inv_ready[b], through(g, 2) - 1 + half)
                    dve.tensor_tensor(probs[:, b, heads], probs[:, b, heads],
                                      row_inv[:, b, heads].unsqueeze(2).to_broadcast([P, hp, P]),
                                      ALU.mult).then_inc(probs_ready[b], 1)

            def context_lo(g, b):
                dve.wait_ge(ctx_hi[b], through(g))
                dve.tensor_tensor(ctxT[:, LO].rearrange("p c n -> p (c n)"), ps_ctx[:, 0:d],
                                  ctxT[:, HI].rearrange("p c n -> p (c n)").bitcast(F32),
                                  ALU.subtract).then_inc(ctx_lo[b], 1)

            def keys_out(g):
                dve.wait_ge(qk_done[2], through(g))
                if live(g - 1):
                    dve.wait_ge(qk_moved, through(g - 1, 16 * len(moves)))
                for c in (1, 2):
                    e = dve.tensor_scalar(qk_flat[:, K, c, :], ps_work[0][:, (c - 1) * toks:c * toks],
                                          bk_col[:, c:c + 1], None, ALU.add)
                e.then_inc(qk_ready[2], 1)

            def values_out(g):
                for b in range(PAIR):
                    dve.wait_ge(v_done[b], through(g))
                    by_head = ps_work[1 - b][:, 0:d].rearrange("p (h e) -> p h e", e=dh)
                    bias_by_head = rows[:, BV, :].rearrange("p (h e) -> p h e", e=dh)
                    dve.tensor_tensor(v_first[:, b], by_head[:, :, 0:TILE], bias_by_head[:, :, 0:TILE], ALU.add)
                    for side in range(2):
                        e = dve.tensor_tensor(
                            v_rest[:, b, side:HEADS:2, side * rest:(side + 1) * rest],
                            by_head[:, side:HEADS:2, TILE:dh], bias_by_head[:, side:HEADS:2, TILE:dh], ALU.add)
                    e.then_inc(v_ready[b], 1)

            def transposed_lo(g, i, ps_in, hi_ready, xT_out, ready):
                blocks = 2 - i
                dve.wait_ge(hi_ready[i], through(g))
                part = [xT_out[:, p, 2 * i:2 * i + blocks, :].rearrange("p c n -> p (c n)") for p in (HI, LO)]
                dve.tensor_tensor(part[LO], ps_in[:, 0:blocks * toks], part[HI].bitcast(F32),
                                  ALU.subtract).then_inc(ready[i], 1)

            def residual1(g, b, parity):
                if b == 0:
                    dve.wait_ge(x_res_biased, through(g))
                dve.wait_ge(attn_done[b], through(g))
                dve.tensor_tensor(x1[:, parity, b, :], ps_rows[:, 0:d], x_res[:, b, :],
                                  ALU.add).then_inc(res1_ready[b], 1)

            def norm1(g, b, parity):
                dve.wait_ge(rms1_ready[b], through(g))
                dve.scalar_tensor_tensor(out=x1[:, parity, b, :], in0=x1[:, parity, b, :],
                                         scalar=inv_rms1[:, b:b + 1], in1=rows[:, ALPHA1, :],
                                         op0=ALU.mult, op1=ALU.mult).then_inc(x1_scaled[b], 1)
                dve.wait_ge(x1_scaled[b], through(g))
                dve.tensor_tensor(x1[:, parity, b, :], x1[:, parity, b, :], rows[:, GAMMA1, :],
                                  ALU.add).then_inc(x1_ready[b], 1)

            def split_h(g, m):
                hi = h[:, HI, 2 * m:2 * m + 2, :].rearrange("p c n -> p (c n)")
                dve.wait_ge(silu_ready[m], through(g))
                dve.tensor_copy(hi, h_raw[:, m % 2, :]).then_inc(h_hi[m], 1)
                dve.wait_ge(h_hi[m], through(g))
                dve.tensor_tensor(h[:, LO, 2 * m:2 * m + 2, :].rearrange("p c n -> p (c n)"), h_raw[:, m % 2, :],
                                  hi.bitcast(F32), ALU.subtract).then_inc(h_lo[m], 1)

            def residual2(g, b, parity):
                if b == 0:
                    dve.wait_ge(x1_b2_ready, through(g))
                    if live(g - 1):
                        dve.wait_ge(y_stored, through(g - 1, 16))
                dve.wait_ge(down_done[b], through(g))
                dve.tensor_tensor(y[:, b, :], ps_rows[:, 0:d], x1[:, parity, b, :],
                                  ALU.add).then_inc(res2_ready[b], 1)

            def norm2_and_stats(g, b):
                dve.wait_ge(rms2_ready[b], through(g))
                dve.scalar_tensor_tensor(out=y[:, b, :], in0=y[:, b, :], scalar=inv_rms2[:, b:b + 1],
                                         in1=rows[:, ALPHA2, :], op0=ALU.mult,
                                         op1=ALU.mult).then_inc(y_scaled[b], 1)
                dve.wait_ge(y_scaled[b], through(g))
                if b == 0:
                    dve.wait_ge(x_last_biased, through(g))
                dve.tensor_tensor(y[:, b, :], y[:, b, :], x_last[:, b, :], ALU.add).then_inc(y_summed[b], 1)
                dve.wait_ge(y_summed[b], through(g))
                dve.bn_stats(stats[:, b, :], y[:, b, :]).then_inc(stats_ready[b], 1)
                dve.wait_ge(vectors_loaded, 16 * n_vectors)
                dve.wait_ge(stats_ready[b], through(g))
                dve.bn_aggr(mean_var[:, b, :], stats[:, b, :]).then_inc(var_ready[b], 1)

            def layer_norm(g, b):
                dve.wait_ge(std_ready[b], through(g))
                dve.tensor_scalar(y[:, b, :], y[:, b, :], mean_var[:, b, 0:1], inv_std[:, b:b + 1],
                                  ALU.subtract, ALU.mult).then_inc(y_ready[b], 1)

            def slot_program(t, parity):
                g_proj, g_attn, g_ff1, g_ff2 = t - LAG_PROJ, t - LAG_ATTN, t - LAG_FF1, t - LAG_FF2
                if live(g_attn):
                    bias_and_max(g_attn, 0, parity)
                    normalise(g_attn, 0)
                    weights_lo(t, 0)
                if live(g_ff2):
                    residual2(g_ff2, 0, parity)
                if live(g_attn):
                    bias_and_max(g_attn, 1, parity)
                if live(g_ff2):
                    norm2_and_stats(g_ff2, 0)
                if live(g_attn):
                    normalise(g_attn, 1)
                    weights_lo(t, 1)
                if live(g_ff2):
                    layer_norm(g_ff2, 0)
                    residual2(g_ff2, 1, parity)
                if live(g_attn):
                    context_lo(g_attn, 0)
                    weights_lo(t, 2)
                if live(g_ff2):
                    norm2_and_stats(g_ff2, 1)
                if live(g_proj):
                    keys_out(g_proj)
                if live(g_ff2):
                    layer_norm(g_ff2, 1)
                if live(g_attn):
                    residual1(g_attn, 0, parity)
                    context_lo(g_attn, 1)
                    weights_lo(t, 3)
                if live(g_proj):
                    values_out(g_proj)
                if live(t):
                    transposed_lo(t, 0, ps_work[1], xT_hi, xT, xT_lo)
                if live(g_attn):
                    norm1(g_attn, 0, parity)
                    residual1(g_attn, 1, parity)
                    weights_lo(t, 4)
                if live(t):
                    transposed_lo(t, 1, ps_ctx, xT_hi, xT, xT_lo)
                weights_lo(t, 5)
                if static(t) and t == 0:
                    scale_query_bias()
                for m in range(fc // 2):
                    if live(g_ff1):
                        split_h(g_ff1, m)
                    if live(g_attn) and m == 1:
                        norm1(g_attn, 1, parity)
                if live(g_attn):
                    transposed_lo(g_attn, 0, ps_work[0], x1T_hi, x1T, x1T_lo)
                    transposed_lo(g_attn, 1, ps_ctx, x1T_hi, x1T, x1T_lo)

            run_slots(dve, slot_program)


_INS = ["x", "adj"] + ["L0_gnn_" + n for n in (
    "wq", "bq", "wk", "bk", "wv", "bv", "wo", "bo", "w1", "b1", "w2", "b2",
    "alpha1", "gamma1", "alpha2", "gamma2")]


def kernel(**inputs):
    import numpy as _np
    import concourse.bacc as _bacc
    from concourse import mybir as _mybir
    from concourse.bass_utils import run_bass_kernel_spmd as _run

    nc = _bacc.Bacc("TRN2", target_bir_lowering=False, num_devices=1, dynamic_dma_scratch_size=1024)
    arrays, args = {}, []
    for name in _INS:
        a = _np.ascontiguousarray(inputs[name])
        arrays[f"in_{name}"] = a
        args.append(nc.dram_tensor(f"in_{name}", a.shape, _mybir.dt.from_np(a.dtype), kind="ExternalInput").ap())
    args.append(nc.dram_tensor("out", inputs["x"].shape, F32, kind="ExternalOutput").ap())
    build_layer(nc, *args)
    r = _run(nc, [arrays], core_ids=[0])
    return r.results[0]["out"]
```
